# Optimizing a Trainium2 kernel written in Bass

```python
import numpy as np
import jax
import jax.numpy as jnp

def _softmax(x, axis=-1):
    return jax.nn.softmax(x, axis=axis)
def _gelu(x):
    return jax.nn.gelu(x, approximate=True)
def _silu(x):
    return jax.nn.silu(x)
def _sigmoid(x):
    return jax.nn.sigmoid(x)
def _layernorm(x, axis=-1, eps=1e-5):
    m = jnp.mean(x, axis=axis, keepdims=True)
    v = jnp.var(x, axis=axis, keepdims=True)
    return (x - m) / jnp.sqrt(v + eps)
def _scatter_add(tgt, idx, src, axis=0):
    return tgt.at[idx].add(src)
def _segment_sum(src, seg, n):
    return jax.ops.segment_sum(src, seg, n)

kernel_name = 'mk_conv_preact_d2_conv_nhwc512_5986df'

def setup_inputs(seed: int = 0):
    np.random.seed(seed)
    _w = jnp.asarray
    def _rec_inputs():
        import jax
        import jax.numpy as jnp
        _gk = jax.random.key(seed)
        x = -0.000125 + 0.9999 * jax.random.normal(jax.random.fold_in(_gk, 1), (8, 64, 128, 512), jnp.float32)
        return x
    x = _rec_inputs()
    def _L0_conv_setup():
        import jax, jax.numpy as jnp
        import numpy as np
        B, T1, T2, D, O = (8, 64, 128, 512, 512)
        key = jax.random.key(seed)
        k1, k2, k3 = jax.random.split(key, 3)
        X = jax.random.normal(k1, (B, T1, T2, D), dtype=jnp.float32)
        W = jax.random.normal(k2, (D, O), dtype=jnp.float32) * (1.0 / np.sqrt(D))
        b = jax.random.normal(k3, (O,), dtype=jnp.float32) * 0.01
        return {'X': X, 'W': W, 'b': b}
    _L0_conv_all = _L0_conv_setup()
    _L0_conv_in = {k: v for k, v in _L0_conv_all.items() if k in ('W', 'b', )}
    del _L0_conv_all

    def _L1_conv_setup():
        import jax, jax.numpy as jnp
        import numpy as np
        B, T1, T2, D, O = (8, 64, 128, 512, 512)
        key = jax.random.key(seed)
        k1, k2, k3 = jax.random.split(key, 3)
        X = jax.random.normal(k1, (B, T1, T2, D), dtype=jnp.float32)
        W = jax.random.normal(k2, (D, O), dtype=jnp.float32) * (1.0 / np.sqrt(D))
        b = jax.random.normal(k3, (O,), dtype=jnp.float32) * 0.01
        return {'X': X, 'W': W, 'b': b}
    _L1_conv_all = _L1_conv_setup()
    _L1_conv_in = {k: v for k, v in _L1_conv_all.items() if k in ('W', 'b', )}
    del _L1_conv_all

    return {
        "x": x,
        "L0_conv_W": _L0_conv_in["W"],
        "L0_conv_b": _L0_conv_in["b"],
        "L1_conv_W": _L1_conv_in["W"],
        "L1_conv_b": _L1_conv_in["b"],
    }

def reference(x, L0_conv_W, L0_conv_b, L1_conv_W, L1_conv_b):
    import jax
    import jax.numpy as jnp
    def _L0_conv_ref(X, W, b):
        import jax, jax.numpy as jnp
        import numpy as np
        B, T1, T2, D, O = (8, 64, 128, 512, 512)
        return jnp.tanh(jnp.einsum('btsd,do->btso', X, W) + b)

    def _L1_conv_ref(X, W, b):
        import jax, jax.numpy as jnp
        import numpy as np
        B, T1, T2, D, O = (8, 64, 128, 512, 512)
        return jnp.tanh(jnp.einsum('btsd,do->btso', X, W) + b)

    def _gn(v, G=32, eps=1e-5):
        B_, H_, W_, C_ = v.shape
        g = v.reshape(B_, H_, W_, G, C_ // G)
        m = jnp.mean(g, axis=(1, 2, 4), keepdims=True)
        s = jnp.var(g, axis=(1, 2, 4), keepdims=True)
        return ((g - m) / jnp.sqrt(s + eps)).reshape(v.shape)

    def _ln_c(v, eps=1e-6):
        m = jnp.mean(v, axis=-1, keepdims=True)
        s = jnp.var(v, axis=-1, keepdims=True)
        return (v - m) / jnp.sqrt(s + eps)

    def _ln_t(v, eps=1e-5):
        m = jnp.mean(v, axis=-1, keepdims=True)
        s = jnp.var(v, axis=-1, keepdims=True)
        return (v - m) / jnp.sqrt(s + eps)

    def _to_tokens(v):
        B_, H_, W_, C_ = v.shape
        return v.reshape(B_, H_ * W_, C_)
    def _from_tokens(t, like):
        return t.reshape(like.shape)

    x = x + _L0_conv_ref(_gn(x), L0_conv_W, L0_conv_b)
    x = x + _L1_conv_ref(_gn(x), L1_conv_W, L1_conv_b)
    return x


_drawn_inputs = setup_inputs


def setup_inputs(seed=0):
    import zlib

    import numpy as np

    out = dict(_drawn_inputs(seed))
    spreads = {}
    factors = {'L0_conv_b': 8.0, 'L1_conv_b': 8.0}
    for name, (base, spread) in spreads.items():
        noise = np.random.default_rng([zlib.crc32(name.encode()), seed]).standard_normal(out[name].shape)
        drawn = base * np.exp(spread * noise) if base else spread * noise
        out[name] = jnp.asarray(drawn.astype(out[name].dtype))
    for name, factor in factors.items():
        out[name] = (out[name] * factor).astype(out[name].dtype)
    return out
```

```python
from contextlib import ExitStack

import concourse.bass as bass
from concourse import mybir

F32 = mybir.dt.float32
F32R = mybir.dt.float32r
ALU = mybir.AluOpType
ACT = mybir.ActivationFunctionType

P = 128
IMAGES, HEIGHT, WIDTH, CHANNELS = 8, 64, 128, 512
GROUPS = 32
PER_GROUP = CHANNELS // GROUPS
EPS = 1e-5
LAYERS = 2

TOKENS = HEIGHT * WIDTH
KT = CHANNELS // P
CHUNK = 512
CHUNKS = TOKENS // CHUNK
TB = CHUNK // P
UNITS = LAYERS * CHUNKS
LAST = CHUNKS - 1
STEPS = KT * KT
BN = 6
BASE = 1


def preact_conv_stack(nc, x, w0, b0, w1, b1, out):
    x_rows = x.rearrange("n h w c -> n (h w) c").rearrange("n (p j t) c -> n j p t c", p=P, t=TB)
    out_rows = out.rearrange("n h w c -> n (h w) c").rearrange("n (p j t) c -> n j p t c", p=P, t=TB)

    with ExitStack() as ctx:
        def sb(name, shape, dt=F32):
            return ctx.enter_context(nc.sbuf_tensor(name, shape, dt))

        def psum(name, shape):
            return ctx.enter_context(nc.psum_tensor(name, shape, F32))

        def sem(name):
            return ctx.enter_context(nc.semaphore(name))

        ring = sb("ring", [P, CHUNKS, KT, CHUNK])
        w_hi = sb("w_hi", [P, LAYERS, KT, CHANNELS], F32R)
        w_lo = sb("w_lo", [P, LAYERS, KT, CHANNELS], F32R)
        x_hi = sb("x_hi", [P, KT, CHUNK], F32R)
        x_lo = sb("x_lo", [P, KT, CHUNK], F32R)
        xn = sb("xn", [P, 2, CHUNK])
        th = sb("th", [P, 2, CHUNK])
        y = sb("y", [P, KT, CHUNK])
        rows_in = sb("rows_in", [P, 2, TB, CHANNELS])
        rows_out = sb("rows_out", [P, 2, TB // 2, CHANNELS])
        bias = sb("bias", [P, LAYERS, KT])
        ident = sb("ident", [P, P])
        group_mean = sb("group_mean", [P, P])
        stats = sb("stats", [P, LAYERS, KT, CHUNKS * BN])
        agg = sb("agg", [P, KT, 2])
        mean = sb("mean", [P, KT])
        diff = sb("diff", [P, KT])
        spread = sb("spread", [P, KT])
        var_eps = sb("var_eps", [P, KT])
        power = sb("power", [P, 1])
        rstd = sb("rstd", [P, KT])
        w_raw = [y, rows_out[:, :, :, :].rearrange("p a t c -> p (a t) c")]

        acc = [psum(f"acc{o}", [P, CHUNK]) for o in range(KT)]
        turn_in = [psum(f"turn_in{i}", [P, CHUNK]) for i in range(2)]
        turn_out = psum("turn_out", [P, CHANNELS])
        small = psum("small", [P, CHUNK])

        zeroed = sem("zeroed")
        consts = sem("consts")
        w_come = [sem(f"w_come{l}") for l in range(LAYERS)]
        bias_come = sem("bias_come")
        w_high = sem("w_high")
        w_split = sem("w_split")
        rows_come = [sem(f"rows_come{i}") for i in range(2)]
        stored = [sem(f"stored{i}") for i in range(2)]
        turned_in = sem("turned_in")
        ring_filled = sem("ring_filled")
        turned_out = sem("turned_out")
        out_copied = sem("out_copied")
        xn_ready = sem("xn_ready")
        hi_ready = sem("hi_ready")
        lo_ready = sem("lo_ready")
        steps_done = sem("steps_done")
        tanh_done = sem("tanh_done")
        added = sem("added")
        stats_done = sem("stats_done")
        agg_ready = sem("agg_ready")
        mean_done = sem("mean_done")
        mean_kept = sem("mean_kept")
        diff_ready = sem("diff_ready")
        spread_ready = sem("spread_ready")
        spread_done = sem("spread_done")
        var_ready = sem("var_ready")
        rstd_ready = sem("rstd_ready")

        def used(u, k, by_output):
            return STEPS * u + ((KT - 1) * KT + k + 1 if by_output else KT * (k + 1))

        def summed(u, o, by_output):
            return STEPS * u + (KT * (o + 1) if by_output else (KT - 1) * KT + o + 1)

        block = ctx.enter_context(nc.Block())

        @block.sync
        def _(sp):
            def load(n, c, half, wait=True):
                if wait:
                    sp.wait_ge(turned_in, KT * (CHUNKS * n + c - 1))
                sp.dma_start(rows_in[:, half], x_rows[n, c]).then_inc(rows_come[half], 16)

            def store(n, c):
                for h in range(2):
                    sp.wait_ge(out_copied, BASE + TB * (CHUNKS * n + c) + 2 * h + 2)
                    sp.dma_start(out_rows[n, c, :, 2 * h:2 * h + 2], rows_out[:, h])\
                        .then_inc(stored[h], 16)

            for h in range(2):
                sp.sem_inc(stored[h], BASE)
            for c in range(2):
                load(0, c, c, wait=False)
            for l, (w, b) in enumerate(((w0, b0), (w1, b1))):
                sp.dma_start(w_raw[l][:, :, :], w.rearrange("(k p) o -> p k o", p=P)).then_inc(w_come[l], 16)
                with nc.allow_non_contiguous_dma(reason="one bias value per partition"):
                    sp.dma_start(bias[:, l, :], b.rearrange("(o p) -> p o", p=P)).then_inc(bias_come, 16)
            with sp.Fori(1, CHUNKS // 2) as pair:
                for h in range(2):
                    load(0, 2 * pair + h, h)
            with sp.Fori(0, IMAGES - 1) as n:
                for c in range(2):
                    load(n + 1, c, c)
                with sp.Fori(0, CHUNKS // 2 - 1) as pair:
                    for h in range(2):
                        store(n, 2 * pair + h)
                        load(n + 1, 2 * pair + h + 2, h)
                for c in range(CHUNKS - 2, CHUNKS):
                    store(n, c)
            with sp.Fori(0, CHUNKS) as c:
                store(IMAGES - 1, c)
            for h in range(2):
                sp.wait_ge(stored[h], BASE + 16 * IMAGES * CHUNKS)

        @block.gpsimd
        def _(pool):
            pool.memset(ident[:, :], 0.0).then_inc(zeroed, 1)
            pool.memset(group_mean[:, :], 1.0 / PER_GROUP).then_inc(zeroed, 1)
            pool.memset(power[:, :], -0.5).then_inc(consts, 1)
            pool.wait_ge(zeroed, 2)
            pool.affine_select(out=ident[:, :], in_=ident[:, :], compare_op=ALU.not_equal, fill=1.0,
                               base=0, pattern=[[-1, P]], channel_multiplier=1).then_inc(consts, 1)
            blocks = group_mean[:, :].rearrange("p (g i) -> p g i", i=PER_GROUP)
            pool.affine_select(out=blocks, in_=blocks, compare_op=ALU.is_ge, fill=0.0, base=0,
                               pattern=[[-PER_GROUP, P // PER_GROUP], [0, PER_GROUP]],
                               channel_multiplier=1).then_inc(zeroed, 1)
            pool.wait_ge(zeroed, 3)
            pool.affine_select(out=blocks, in_=blocks, compare_op=ALU.is_ge, fill=0.0, base=PER_GROUP - 1,
                               pattern=[[PER_GROUP, P // PER_GROUP], [0, PER_GROUP]],
                               channel_multiplier=-1).then_inc(consts, 1)
            pool.wait_ge(consts, 1)
            with pool.Fori(0, IMAGES * LAYERS) as s:
                for k in range(KT):
                    pool.wait_ge(var_ready, KT * s + k + 1)
                    pool.tensor_tensor(rstd[:, k:k + 1], var_eps[:, k:k + 1], power[:, :], ALU.pow)\
                        .then_inc(rstd_ready, 1)

        @block.tensor
        def _(pe):
            def step(u, layer, by_output, s, first=False):
                o, k = divmod(s, KT) if by_output else (s % KT, s // KT)
                if (by_output and o == 0) or (not by_output and o == 0):
                    pe.wait_ge(lo_ready, KT * u + k + 1)
                if k == 0 and not first:
                    pe.wait_ge(tanh_done, KT * (u - 1) + o + 1)
                cols = slice(o * P, (o + 1) * P)
                pe.matmul(acc[o][:, :], w_lo[:, layer, k, cols], x_hi[:, k], start=(k == 0), stop=False)
                pe.matmul(acc[o][:, :], w_hi[:, layer, k, cols], x_lo[:, k], start=False, stop=False)
                pe.matmul(acc[o][:, :], w_hi[:, layer, k, cols], x_hi[:, k], start=False,
                          stop=(k == KT - 1)).then_inc(steps_done, 1)

            def bring_in(n, c, half, k, first=False):
                if k == 0:
                    pe.wait_ge(rows_come[half], 8 * (CHUNKS * n + c - half) + 16)
                if not first:
                    pe.wait_ge(ring_filled, KT * (CHUNKS * n + c) + k - 1)
                for t in range(TB):
                    mm = pe.transpose(turn_in[k % 2][:, t * P:(t + 1) * P],
                                      rows_in[:, half, t, k * P:(k + 1) * P], ident[:, :])
                mm.then_inc(turned_in, 1)

            def take_out(n, c, t):
                if t == 0:
                    pe.wait_ge(added, KT * (UNITS * n + CHUNKS + c + 1))
                pe.wait_ge(out_copied, BASE + TB * (CHUNKS * n + c) + t)
                for k in range(KT):
                    mm = pe.transpose(turn_out[:, k * P:(k + 1) * P], y[:, k, t * P:(t + 1) * P], ident[:, :])
                mm.then_inc(turned_out, 1)

            def mean_over_group(stage, k):
                pe.wait_ge(agg_ready, KT * stage + k + 1)
                pe.wait_ge(var_ready, KT * stage + k)
                pe.matmul(small[:, k:k + 1], group_mean[:, :], agg[:, k, 0:1], start=True, stop=True)\
                    .then_inc(mean_done, 1)

            def spread_over_group(stage, k):
                pe.wait_ge(spread_ready, KT * stage + k + 1)
                pe.matmul(small[:, KT + k:KT + k + 1], group_mean[:, :], spread[:, k:k + 1],
                          start=True, stop=True).then_inc(spread_done, 1)

            def unit(u, layer, by_output, between, first=False):
                for s in range(STEPS):
                    step(u, layer, by_output, s, first)
                    for what, *args in between.get(s, ()):
                        what(*args)

            def middle(n, layer, incoming):
                with pe.Fori(0, CHUNKS // 2 - 1) as pair:
                    for h in range(2):
                        j = 2 * pair + h + 1
                        c = j - 1
                        between = {}
                        if layer == 1:
                            between = {2 + 2 * t: [(take_out, n, c, t)] for t in range(TB)}
                            if incoming:
                                for k in range(KT):
                                    between[3 + 2 * k] = [(bring_in, n + 1, c, h, k)]
                        unit(UNITS * n + CHUNKS * layer + j, layer, False, between)

            def layer0_first(n, first=False):
                between = {}
                if not first:
                    stage = LAYERS * n
                    between = {2 + 2 * t: [(take_out, n - 1, LAST, t)] for t in range(TB)}
                    between[0] = [(spread_over_group, stage, 2)]
                    between[4].append((mean_over_group, stage, 3))
                    between[5] = [(spread_over_group, stage, 3)]
                unit(UNITS * n, 0, False, between, first)

            def layer0_rest(n):
                middle(n, 0, False)
                stage = LAYERS * n + 1
                unit(UNITS * n + LAST, 0, True,
                     {7: [(mean_over_group, stage, 0)], 8: [(spread_over_group, stage, 0)],
                      11: [(mean_over_group, stage, 1)], 12: [(spread_over_group, stage, 1)],
                      15: [(mean_over_group, stage, 2)]})

            def layer1(n, incoming):
                stage = LAYERS * n + 1
                unit(UNITS * n + CHUNKS, 1, False,
                     {0: [(spread_over_group, stage, 2)], 3: [(mean_over_group, stage, 3)],
                      4: [(spread_over_group, stage, 3)]})
                middle(n, 1, incoming)
                between = {2 + t: [(take_out, n, LAST - 1, t)] for t in range(TB)}
                if incoming:
                    stage = LAYERS * (n + 1)
                    between[5].append((bring_in, n + 1, LAST - 1, 0, 0))
                    between[6] = [(bring_in, n + 1, LAST - 1, 0, 1)]
                    between[7] = [(bring_in, n + 1, LAST - 1, 0, 2)]
                    between[8] = [(bring_in, n + 1, LAST - 1, 0, 3)]
                    between[9] = [(bring_in, n + 1, LAST, 1, 0)]
                    between[10] = [(bring_in, n + 1, LAST, 1, 1), (mean_over_group, stage, 0)]
                    between[11] = [(spread_over_group, stage, 0)]
                    between[12] = [(bring_in, n + 1, LAST, 1, 2), (mean_over_group, stage, 1)]
                    between[13] = [(spread_over_group, stage, 1)]
                    between[14] = [(bring_in, n + 1, LAST, 1, 3)]
                    between[15] = [(mean_over_group, stage, 2)]
                unit(UNITS * n + CHUNKS + LAST, 1, True, between)

            pe.sem_inc(turned_out, BASE)
            pe.wait_ge(consts, 3)
            for c in range(2):
                for k in range(KT):
                    bring_in(0, c, c, k, first=(c == 0 and k < 2))
            with pe.Fori(1, CHUNKS // 2) as pair:
                for h in range(2):
                    for k in range(KT):
                        bring_in(0, 2 * pair + h, h, k)
            for k in range(KT):
                mean_over_group(0, k)
                spread_over_group(0, k)
            pe.wait_ge(w_split, LAYERS)
            layer0_first(0, first=True)
            with pe.Fori(0, IMAGES - 1) as n:
                layer0_rest(n)
                layer1(n, True)
                layer0_first(n + 1)
            layer0_rest(IMAGES - 1)
            layer1(IMAGES - 1, False)
            for t in range(TB):
                take_out(IMAGES - 1, LAST, t)

        @block.scalar
        def _(act):
            def high(u, k, by_output, first=False):
                act.wait_ge(xn_ready, KT * u + k + 1)
                if not first:
                    act.wait_ge(steps_done, used(u - 1, k, by_output))
                act.activation(x_hi[:, k], xn[:, k % 2], ACT.Copy).then_inc(hi_ready, 1)

            def squash(u, layer, o, by_output):
                act.wait_ge(steps_done, summed(u, o, by_output))
                if by_output or o >= 2:
                    act.wait_ge(added, KT * u + o - 1)
                act.activation(th[:, o % 2], acc[o][:, :], ACT.Tanh, bias=bias[:, layer, o:o + 1])\
                    .then_inc(tanh_done, 1)

            def fill_ring(n, c, k, first=False):
                act.wait_ge(turned_in, KT * (CHUNKS * n + c) + k + 1)
                if not first:
                    act.wait_ge(added, KT * (UNITS * (n - 1) + CHUNKS + c) + k + 1)
                act.activation(ring[:, c, k], turn_in[k % 2][:, :], ACT.Copy).then_inc(ring_filled, 1)

            def copy_out(n, c, t):
                act.wait_ge(turned_out, BASE + TB * (CHUNKS * n + c) + t + 1)
                if t % 2 == 0:
                    act.wait_ge(stored[t // 2], BASE + 16 * (CHUNKS * n + c))
                act.activation(rows_out[:, t // 2, t % 2], turn_out[:, :], ACT.Copy).then_inc(out_copied, 1)

            def finish_last(u, layer):
                for o in range(KT - 1):
                    squash(u - 1, layer, o, False)
                high(u, KT - 1, False)
                squash(u - 1, layer, KT - 1, False)

            def middle(n, layer, incoming):
                def one(u, c):
                    finish_last(u, layer)
                    for k in range(KT - 1):
                        if layer == 1:
                            for t in ((0, 1), (2, 3), ())[k]:
                                copy_out(n, c, t)
                                if incoming:
                                    fill_ring(n + 1, c, t)
                        high(u + 1, k, False)
                with act.Fori(0, CHUNKS // 2 - 1) as pair:
                    for h in range(2):
                        one(UNITS * n + CHUNKS * layer + 2 * pair + h + 1, 2 * pair + h)

            def layer0_first(n, first=False):
                u = UNITS * n
                if not first:
                    for t in range(TB - 1):
                        copy_out(n - 1, LAST, t)
                high(u, KT - 1, True, first)
                if not first:
                    copy_out(n - 1, LAST, TB - 1)
                for k in range(KT - 1):
                    high(u + 1, k, False)

            def layer0_rest(n):
                middle(n, 0, False)
                u = UNITS * n + LAST
                finish_last(u, 0)
                squash(u, 0, 0, True)
                squash(u, 0, 1, True)
                squash(u, 0, 2, True)
                high(u + 1, 0, True)
                high(u + 1, 1, True)
                squash(u, 0, 3, True)
                high(u + 1, 2, True)

            def layer1(n, incoming):
                u = UNITS * n + CHUNKS
                high(u, KT - 1, True)
                for k in range(KT - 1):
                    high(u + 1, k, False)
                middle(n, 1, incoming)
                u = u + LAST
                finish_last(u, 1)
                copy_out(n, LAST - 1, 0)
                copy_out(n, LAST - 1, 1)
                squash(u, 1, 0, True)
                copy_out(n, LAST - 1, 2)
                copy_out(n, LAST - 1, 3)
                if incoming:
                    for k in range(3):
                        fill_ring(n + 1, LAST - 1, k)
                squash(u, 1, 1, True)
                if incoming:
                    fill_ring(n + 1, LAST - 1, 3)
                    fill_ring(n + 1, LAST, 0)
                    fill_ring(n + 1, LAST, 1)
                squash(u, 1, 2, True)
                if incoming:
                    high(u + 1, 0, True)
                    fill_ring(n + 1, LAST, 2)
                    high(u + 1, 1, True)
                squash(u, 1, 3, True)
                if incoming:
                    fill_ring(n + 1, LAST, 3)
                    high(u + 1, 2, True)

            act.sem_inc(out_copied, BASE)
            act.wait_ge(bias_come, 16 * LAYERS)
            with act.Fori(0, CHUNKS) as c:
                for k in range(KT):
                    fill_ring(0, c, k, first=True)
            for k in range(KT - 1):
                high(0, k, True, first=True)
            layer0_first(0, first=True)
            with act.Fori(0, IMAGES - 1) as n:
                layer0_rest(n)
                layer1(n, True)
                layer0_first(n + 1)
            layer0_rest(IMAGES - 1)
            layer1(IMAGES - 1, False)
            for t in range(TB):
                copy_out(IMAGES - 1, LAST, t)

        @block.vector
        def _(dve):
            def normalize(u, chunk, k, first=False):
                if not first:
                    dve.wait_ge(lo_ready, KT * u + k - 1)
                dve.tensor_scalar(xn[:, k % 2], ring[:, chunk, k], mean[:, k:k + 1], rstd[:, k:k + 1],
                                  ALU.subtract, ALU.mult).then_inc(xn_ready, 1)

            def low(u, k):
                dve.wait_ge(hi_ready, KT * u + k + 1)
                dve.tensor_tensor(x_lo[:, k], xn[:, k % 2], x_hi[:, k].bitcast(F32), ALU.subtract)\
                    .then_inc(lo_ready, 1)

            def add(u, n, layer, chunk, o):
                dve.wait_ge(tanh_done, KT * u + o + 1)
                if layer == 0:
                    dve.tensor_tensor(ring[:, chunk, o], ring[:, chunk, o], th[:, o % 2], ALU.add)\
                        .then_inc(added, 1)
                else:
                    dve.wait_ge(turned_out, BASE + TB * (CHUNKS * n + chunk))
                    dve.tensor_tensor(y[:, o], ring[:, chunk, o], th[:, o % 2], ALU.add).then_inc(added, 1)

            def stats_of_sum(u, n, chunk, o):
                dve.wait_ge(added, KT * u + o + 1)
                dve.bn_stats(stats[:, 1, o, bass.ds(chunk * BN, BN)], ring[:, chunk, o]).then_inc(stats_done, 1)

            def stats_of_input(n, chunk, k):
                dve.wait_ge(ring_filled, KT * (CHUNKS * n + chunk) + k + 1)
                dve.bn_stats(stats[:, 0, k, bass.ds(chunk * BN, BN)], ring[:, chunk, k]).then_inc(stats_done, 1)

            def aggregate(stage, layer, k):
                dve.drain()
                dve.bn_aggr(agg[:, k], stats[:, layer, k]).then_inc(agg_ready, 1)

            def group_mean_and_spread(stage, k):
                dve.wait_ge(mean_done, KT * stage + k + 1)
                dve.tensor_copy(mean[:, k:k + 1], small[:, k:k + 1]).then_inc(mean_kept, 1)
                dve.wait_ge(mean_kept, KT * stage + k + 1)
                dve.tensor_tensor(diff[:, k:k + 1], agg[:, k, 0:1], mean[:, k:k + 1], ALU.subtract)\
                    .then_inc(diff_ready, 1)
                dve.wait_ge(diff_ready, KT * stage + k + 1)
                dve.scalar_tensor_tensor(spread[:, k:k + 1], diff[:, k:k + 1], diff[:, k:k + 1],
                                         agg[:, k, 1:2], ALU.mult, ALU.add).then_inc(spread_ready, 1)

            def group_variance(stage, k):
                dve.wait_ge(spread_done, KT * stage + k + 1)
                dve.tensor_scalar(var_eps[:, k:k + 1], small[:, KT + k:KT + k + 1], EPS, None, ALU.add)\
                    .then_inc(var_ready, 1)

            def normalize_first(u, stage, k, first=False):
                dve.wait_ge(rstd_ready, KT * stage + k + 1)
                normalize(u, 0, k, first)

            def finish_last(u, n, layer, chunk):
                for o in range(KT):
                    add(u - 1, n, layer, chunk - 1, o)
                    if layer == 0:
                        stats_of_sum(u - 1, n, chunk - 1, o)
                    if o == 1:
                        low(u, KT - 1)

            def ahead(u, chunk, between=((), (), ())):
                normalize(u + 1, chunk + 1, 0)
                normalize(u + 1, chunk + 1, 1)
                for k in range(KT - 1):
                    low(u + 1, k)
                    for args in between[k]:
                        stats_of_input(*args)
                    if k + 2 < KT:
                        normalize(u + 1, chunk + 1, k + 2)

            def middle(n, layer, incoming):
                with dve.Fori(0, CHUNKS // 2 - 1) as pair:
                    for h in range(2):
                        c = 2 * pair + h + 1
                        u = UNITS * n + CHUNKS * layer + c
                        finish_last(u, n, layer, c)
                        if layer == 1 and incoming:
                            ahead(u, c, (((n + 1, c - 1, 0), (n + 1, c - 1, 1)),
                                         ((n + 1, c - 1, 2), (n + 1, c - 1, 3)), ()))
                        else:
                            ahead(u, c)

            def layer0_first(n):
                low(UNITS * n, KT - 1)
                ahead(UNITS * n, 0)

            def layer0_rest(n):
                middle(n, 0, False)
                u, stage = UNITS * n + LAST, LAYERS * n + 1
                finish_last(u, n, 0, LAST)
                for k in range(2):
                    add(u, n, 0, LAST, k)
                    stats_of_sum(u, n, LAST, k)
                    aggregate(stage, 1, k)
                    group_mean_and_spread(stage, k)
                    group_variance(stage, k)
                    normalize_first(u + 1, stage, k)
                add(u, n, 0, LAST, 2)
                stats_of_sum(u, n, LAST, 2)
                aggregate(stage, 1, 2)
                low(u + 1, 0)
                low(u + 1, 1)
                group_mean_and_spread(stage, 2)
                group_variance(stage, 2)
                normalize_first(u + 1, stage, 2)
                add(u, n, 0, LAST, 3)
                stats_of_sum(u, n, LAST, 3)
                aggregate(stage, 1, 3)
                low(u + 1, 2)
                group_mean_and_spread(stage, 3)
                group_variance(stage, 3)
                normalize_first(u + 1, stage, 3)

            def layer1(n, incoming):
                u = UNITS * n + CHUNKS
                low(u, KT - 1)
                ahead(u, 0)
                middle(n, 1, incoming)
                u, stage = u + LAST, LAYERS * (n + 1)
                finish_last(u, n, 1, LAST)
                add(u, n, 1, LAST, 0)
                if incoming:
                    for k in range(3):
                        stats_of_input(n + 1, LAST - 1, k)
                add(u, n, 1, LAST, 1)
                if incoming:
                    stats_of_input(n + 1, LAST - 1, 3)
                    for k in range(2):
                        stats_of_input(n + 1, LAST, k)
                        aggregate(stage, 0, k)
                    for k in range(2):
                        group_mean_and_spread(stage, k)
                        group_variance(stage, k)
                        normalize_first(u + 1, stage, k)
                add(u, n, 1, LAST, 2)
                if incoming:
                    low(u + 1, 0)
                    stats_of_input(n + 1, LAST, 2)
                    aggregate(stage, 0, 2)
                    low(u + 1, 1)
                add(u, n, 1, LAST, 3)
                if incoming:
                    group_mean_and_spread(stage, 2)
                    group_variance(stage, 2)
                    normalize_first(u + 1, stage, 2)
                    stats_of_input(n + 1, LAST, 3)
                    aggregate(stage, 0, 3)
                    low(u + 1, 2)
                    group_mean_and_spread(stage, 3)
                    group_variance(stage, 3)
                    normalize_first(u + 1, stage, 3)

            for l in range(LAYERS):
                dve.wait_ge(w_come[l], 16)
                dve.tensor_copy(w_hi[:, l], w_raw[l][:, :, :]).then_inc(w_high, 1)
                dve.wait_ge(w_high, l + 1)
                dve.tensor_tensor(w_lo[:, l], w_raw[l][:, :, :], w_hi[:, l].bitcast(F32), ALU.subtract)\
                    .then_inc(w_split, 1)
            with dve.Fori(0, CHUNKS) as c:
                for k in range(KT):
                    stats_of_input(0, c, k)
            for k in range(KT):
                aggregate(0, 0, k)
                group_mean_and_spread(0, k)
                group_variance(0, k)
            normalize_first(0, 0, 0, first=True)
            normalize_first(0, 0, 1, first=True)
            low(0, 0)
            normalize_first(0, 0, 2)
            low(0, 1)
            normalize_first(0, 0, 3)
            low(0, 2)
            layer0_first(0)
            with dve.Fori(0, IMAGES - 1) as n:
                layer0_rest(n)
                layer1(n, True)
                layer0_first(n + 1)
            layer0_rest(IMAGES - 1)
            layer1(IMAGES - 1, False)


def kernel(**inputs):
    import numpy as _np
    import concourse.bacc as _bacc
    from concourse import mybir as _mybir
    from concourse.bass_utils import run_bass_kernel_spmd as _run

    nc = _bacc.Bacc("TRN2", target_bir_lowering=False, num_devices=1, dynamic_dma_scratch_size=1024)
    arrays, args = {}, []
    for name in ("x", "L0_conv_W", "L0_conv_b", "L1_conv_W", "L1_conv_b"):
        a = _np.ascontiguousarray(inputs[name])
        arrays[f"in_{name}"] = a
        args.append(nc.dram_tensor(f"in_{name}", a.shape, _mybir.dt.from_np(a.dtype), kind="ExternalInput").ap())
    shape = (IMAGES, HEIGHT, WIDTH, CHANNELS)
    args.append(nc.dram_tensor("out", shape, _mybir.dt.float32, kind="ExternalOutput").ap())
    preact_conv_stack(nc, *args)
    result = _run(nc, [arrays], core_ids=[0])
    return result.results[0]["out"]
```

```python
from contextlib import ExitStack

import concourse.bass as bass
from concourse import mybir

F32 = mybir.dt.float32
F32R = mybir.dt.float32r
ALU = mybir.AluOpType
ACT = mybir.ActivationFunctionType

P = 128
IMAGES, HEIGHT, WIDTH, CHANNELS = 8, 64, 128, 512
GROUPS = 32
PER_GROUP = CHANNELS // GROUPS
EPS = 1e-5
LAYERS = 2

TOKENS = HEIGHT * WIDTH
KT = CHANNELS // P
CHUNK = 512
CHUNKS = TOKENS // CHUNK
UNITS = LAYERS * CHUNKS
LAST = CHUNKS - 1
STEPS = KT * KT
Q = 32
QUADS = P // Q
BLOCKS = CHUNK // Q
BN = 6
BASE = 1


def preact_conv_stack(nc, x, w0, b0, w1, b1, out):
    def quads(a):
        return a.rearrange("n h w c -> n (h w) c").rearrange("n (j b i) (q d) -> n j q i b d", b=BLOCKS, i=Q, q=QUADS)

    x_quads, out_quads = quads(x), quads(out)

    with ExitStack() as ctx:
        def sb(name, shape, dt=F32):
            return ctx.enter_context(nc.sbuf_tensor(name, shape, dt))

        def psum(name, shape):
            return ctx.enter_context(nc.psum_tensor(name, shape, F32))

        def sem(name):
            return ctx.enter_context(nc.semaphore(name))

        ring = sb("ring", [P, CHUNKS, KT, CHUNK])
        w_hi = sb("w_hi", [P, LAYERS, KT, CHANNELS], F32R)
        w_lo = sb("w_lo", [P, LAYERS, KT, CHANNELS], F32R)
        x_hi = sb("x_hi", [P, KT, CHUNK], F32R)
        x_lo = sb("x_lo", [P, KT, CHUNK], F32R)
        xn = sb("xn", [P, 2, CHUNK])
        th = sb("th", [P, KT, CHUNK])
        rows_in = sb("rows_in", [P, 2, BLOCKS, KT, Q])
        rows_out = sb("rows_out", [P, 2, BLOCKS, KT, Q])
        bias = sb("bias", [P, LAYERS, KT])
        group_mean = sb("group_mean", [P, P])
        stats = sb("stats", [P, KT, CHUNKS * BN])
        agg = sb("agg", [P, KT, 2])
        minus_mean = sb("minus_mean", [P, KT])
        diff = sb("diff", [P, KT])
        spread = sb("spread", [P, KT])
        var_eps = sb("var_eps", [P, KT])
        power = sb("power", [P, 1])
        rstd = sb("rstd", [P, KT])
        shift = sb("shift", [P, KT])
        w_raw = [th[:, :, :], rows_out[:, 0].rearrange("p b k i -> p (b k i)").rearrange("p (k c) -> p k c", k=KT)]

        acc = [psum(f"acc{o}", [P, CHUNK]) for o in range(KT)]
        small = psum("small", [P, CHUNK])

        zeroed = sem("zeroed")
        consts = sem("consts")
        w_come = [sem(f"w_come{l}") for l in range(LAYERS)]
        bias_come = sem("bias_come")
        w_high = sem("w_high")
        w_split = sem("w_split")
        rows_come = [sem(f"rows_come{i}") for i in range(2)]
        stored = [sem(f"stored{i}") for i in range(2)]
        turned_in = sem("turned_in")
        turned_out = sem("turned_out")
        xn_ready = sem("xn_ready")
        hi_ready = sem("hi_ready")
        lo_ready = sem("lo_ready")
        steps_done = sem("steps_done")
        tanh_done = sem("tanh_done")
        added = sem("added")
        agg_ready = sem("agg_ready")
        mean_done = sem("mean_done")
        mean_kept = sem("mean_kept")
        diff_ready = sem("diff_ready")
        spread_ready = sem("spread_ready")
        spread_done = sem("spread_done")
        var_ready = sem("var_ready")
        rstd_ready = sem("rstd_ready")
        shift_ready = sem("shift_ready")

        def used(u, k, by_output):
            return STEPS * u + ((KT - 1) * KT + k + 1 if by_output else KT * (k + 1))

        def summed(u, o, by_output):
            return STEPS * u + (KT * (o + 1) if by_output else (KT - 1) * KT + o + 1)

        def w_parts(l, q):
            raw = w_raw[l].rearrange("p k (q o i) -> p q k o i", q=QUADS, i=Q)[:, q]
            hi, lo = (w[:, l].rearrange("p k (o q i) -> p q k o i", q=QUADS, i=Q)[:, q] for w in (w_hi, w_lo))
            return raw, hi, lo

        block = ctx.enter_context(nc.Block())

        @block.sync
        def _(sp):
            def load(n, c, half, wait=True):
                if wait:
                    sp.wait_ge(turned_in, KT * (CHUNKS * n + c - 1))
                for q in range(QUADS):
                    sp.dma_start(rows_in[Q * q:Q * q + Q, half].rearrange("i b k d -> i b (k d)"),
                                 x_quads[n, c, q]).then_inc(rows_come[half], 16)

            def store(n, c, half):
                sp.wait_ge(turned_out, BASE + KT * (CHUNKS * n + c + 1))
                for q in range(QUADS):
                    sp.dma_start(out_quads[n, c, q], rows_out[Q * q:Q * q + Q, half]
                                 .rearrange("i b k d -> i b (k d)")).then_inc(stored[half], 16)

            for h in range(2):
                sp.sem_inc(stored[h], BASE)
            for c in range(2):
                load(0, c, c, wait=False)
            for l, (w, b) in enumerate(((w0, b0), (w1, b1))):
                w_quads = w.rearrange("(q k i) o -> q i k o", q=QUADS, i=Q)
                b_quads = b.rearrange("(q k i) -> q i k", q=QUADS, i=Q)
                for q in range(QUADS):
                    sp.dma_start(w_raw[l][Q * q:Q * q + Q], w_quads[q]).then_inc(w_come[l], 16)
                    with nc.allow_non_contiguous_dma(reason="one bias value per partition"):
                        sp.dma_start(bias[Q * q:Q * q + Q, l, :], b_quads[q]).then_inc(bias_come, 16)
            with sp.Fori(1, CHUNKS // 2) as pair:
                for h in range(2):
                    load(0, 2 * pair + h, h)
            with sp.Fori(0, IMAGES - 1) as n:
                for c in range(2):
                    load(n + 1, c, c)
                with sp.Fori(0, CHUNKS // 2 - 1) as pair:
                    for h in range(2):
                        store(n, 2 * pair + h, h)
                        load(n + 1, 2 * pair + h + 2, h)
                for c in range(CHUNKS - 2, CHUNKS):
                    store(n, c, c % 2)
            with sp.Fori(0, CHUNKS // 2) as pair:
                for h in range(2):
                    store(IMAGES - 1, 2 * pair + h, h)
            for h in range(2):
                sp.wait_ge(stored[h], BASE + 16 * QUADS * IMAGES * CHUNKS // 2)

        @block.gpsimd
        def _(pool):
            pool.memset(group_mean[:, :], 1.0 / PER_GROUP).then_inc(zeroed, 1)
            pool.memset(power[:, :], -0.5).then_inc(consts, 1)
            pool.wait_ge(zeroed, 1)
            blocks = group_mean[:, :].rearrange("p (g i) -> p g i", i=PER_GROUP)
            pool.affine_select(out=blocks, in_=blocks, compare_op=ALU.is_ge, fill=0.0, base=0,
                               pattern=[[-PER_GROUP, P // PER_GROUP], [0, PER_GROUP]],
                               channel_multiplier=1).then_inc(zeroed, 1)
            pool.wait_ge(zeroed, 2)
            pool.affine_select(out=blocks, in_=blocks, compare_op=ALU.is_ge, fill=0.0, base=PER_GROUP - 1,
                               pattern=[[PER_GROUP, P // PER_GROUP], [0, PER_GROUP]],
                               channel_multiplier=-1).then_inc(consts, 1)
            pool.wait_ge(consts, 1)
            for l in range(LAYERS):
                for q in range(QUADS):
                    raw, hi, lo = w_parts(l, q)
                    pool.wait_ge(w_high, QUADS * l + q + 1)
                    pool.tensor_tensor(lo, raw, hi.bitcast(F32), ALU.subtract).then_inc(w_split, 1)

            def scale_and_shift(stage, k):
                pool.wait_ge(var_ready, KT * stage + k + 1)
                pool.tensor_tensor(rstd[:, k:k + 1], var_eps[:, k:k + 1], power[:, :], ALU.pow)\
                    .then_inc(rstd_ready, 1)
                pool.wait_ge(rstd_ready, KT * stage + k + 1)
                pool.tensor_tensor(shift[:, k:k + 1], minus_mean[:, k:k + 1], rstd[:, k:k + 1], ALU.mult)\
                    .then_inc(shift_ready, 1)

            def add(u, chunk, o):
                pool.wait_ge(tanh_done, KT * u + o + 1)
                pool.tensor_tensor(th[:, o], ring[:, chunk, o], th[:, o], ALU.add).then_inc(added, 1)

            def image(n, more):
                for k in range(KT):
                    scale_and_shift(LAYERS * n + 1, k)
                u = UNITS * n + CHUNKS
                with pool.Fori(0, LAST) as c:
                    for o in range(KT):
                        add(u + c, c, o)
                for o in range(KT):
                    add(u + LAST, LAST, o)
                    if more and o:
                        scale_and_shift(LAYERS * (n + 1), o - 1)
                if more:
                    scale_and_shift(LAYERS * (n + 1), KT - 1)

            for k in range(KT):
                scale_and_shift(0, k)
            with pool.Fori(0, IMAGES - 1) as n:
                image(n, True)
            image(IMAGES - 1, False)

        @block.tensor
        def _(pe):
            def step(u, layer, by_output, s, first=False):
                o, k = divmod(s, KT) if by_output else (s % KT, s // KT)
                if (by_output and o == 0) or (not by_output and o == 0):
                    pe.wait_ge(lo_ready, KT * u + k + 1)
                if k == 0 and not first:
                    pe.wait_ge(tanh_done, KT * (u - 1) + o + 1)
                cols = slice(o * P, (o + 1) * P)
                pe.matmul(acc[o][:, :], w_lo[:, layer, k, cols], x_hi[:, k], start=(k == 0), stop=False)
                pe.matmul(acc[o][:, :], w_hi[:, layer, k, cols], x_lo[:, k], start=False, stop=False)
                pe.matmul(acc[o][:, :], w_hi[:, layer, k, cols], x_hi[:, k], start=False,
                          stop=(k == KT - 1)).then_inc(steps_done, 1)

            def mean_over_group(stage, k):
                pe.wait_ge(agg_ready, KT * stage + k + 1)
                pe.wait_ge(var_ready, KT * stage + k)
                pe.matmul(small[:, k:k + 1], group_mean[:, :], agg[:, k, 0:1], start=True, stop=True)\
                    .then_inc(mean_done, 1)

            def spread_over_group(stage, k):
                pe.wait_ge(spread_ready, KT * stage + k + 1)
                pe.matmul(small[:, KT + k:KT + k + 1], group_mean[:, :], spread[:, k:k + 1],
                          start=True, stop=True).then_inc(spread_done, 1)

            def unit(u, layer, by_output, between, first=False):
                for s in range(STEPS):
                    step(u, layer, by_output, s, first)
                    for what, *args in between.get(s, ()):
                        what(*args)

            def middle(n, layer):
                with pe.Fori(0, CHUNKS // 2 - 1) as pair:
                    for h in range(2):
                        j = 2 * pair + h + 1
                        unit(UNITS * n + CHUNKS * layer + j, layer, False, {})

            def layer0_first(n, first=False):
                between = {}
                if not first:
                    stage = LAYERS * n
                    between = {1: [(mean_over_group, stage, 2)], 2: [(spread_over_group, stage, 2)],
                               5: [(mean_over_group, stage, 3)], 6: [(spread_over_group, stage, 3)]}
                unit(UNITS * n, 0, False, between, first)

            def layer0_rest(n):
                middle(n, 0)
                stage = LAYERS * n + 1
                unit(UNITS * n + LAST, 0, True,
                     {7: [(mean_over_group, stage, 0)], 8: [(spread_over_group, stage, 0)],
                      11: [(mean_over_group, stage, 1)], 12: [(spread_over_group, stage, 1)]})

            def layer1(n, incoming):
                stage = LAYERS * n + 1
                unit(UNITS * n + CHUNKS, 1, False,
                     {0: [(mean_over_group, stage, 2)], 1: [(spread_over_group, stage, 2)],
                      4: [(mean_over_group, stage, 3)], 5: [(spread_over_group, stage, 3)]})
                middle(n, 1)
                between = {}
                if incoming:
                    stage = LAYERS * (n + 1)
                    between = {10: [(mean_over_group, stage, 0)], 12: [(spread_over_group, stage, 0)],
                               13: [(mean_over_group, stage, 1)], 15: [(spread_over_group, stage, 1)]}
                unit(UNITS * n + CHUNKS + LAST, 1, True, between)

            pe.wait_ge(consts, 2)
            for k in range(KT):
                mean_over_group(0, k)
                spread_over_group(0, k)
            pe.wait_ge(w_split, LAYERS * QUADS)
            layer0_first(0, first=True)
            with pe.Fori(0, IMAGES - 1) as n:
                layer0_rest(n)
                layer1(n, True)
                layer0_first(n + 1)
            layer0_rest(IMAGES - 1)
            layer1(IMAGES - 1, False)

        @block.scalar
        def _(act):
            def normalize(u, chunk, k, first=False):
                if not first:
                    act.wait_ge(lo_ready, KT * u + k - 1)
                act.activation(xn[:, k % 2], ring[:, chunk, k], ACT.Identity, bias=shift[:, k:k + 1],
                               scale=rstd[:, k:k + 1]).then_inc(xn_ready, 1)

            def normalize_first(u, stage, k, first=False):
                act.wait_ge(shift_ready, KT * stage + k + 1)
                normalize(u, 0, k, first)

            def high(u, k, by_output, first=False):
                act.wait_ge(xn_ready, KT * u + k + 1)
                if not first:
                    act.wait_ge(steps_done, used(u - 1, k, by_output))
                act.activation(x_hi[:, k], xn[:, k % 2], ACT.Copy).then_inc(hi_ready, 1)

            def squash(u, n, layer, chunk, o, by_output, first=False):
                act.wait_ge(steps_done, summed(u, o, by_output))
                if first:
                    pass
                elif layer == 0:
                    act.wait_ge(added, KT * (u - 1) + o + 1)
                else:
                    act.wait_ge(turned_out, BASE + KT * (CHUNKS * n + chunk - 1) + o + 1)
                act.activation(th[:, o], acc[o][:, :], ACT.Tanh, bias=bias[:, layer, o:o + 1])\
                    .then_inc(tanh_done, 1)

            def middle(n, layer):
                with act.Fori(0, CHUNKS // 2 - 1) as pair:
                    for h in range(2):
                        c = 2 * pair + h + 1
                        u = UNITS * n + CHUNKS * layer + c
                        high(u, KT - 1, False)
                        normalize(u + 1, c + 1, 0)
                        for k in range(KT - 1):
                            normalize(u + 1, c + 1, k + 1)
                            high(u + 1, k, False)
                        for o in range(KT):
                            squash(u, n, layer, c, o, False)

            def first_unit(u, n, layer, first=False):
                high(u, KT - 1, True, first)
                normalize(u + 1, 1, 0)
                for k in range(KT - 1):
                    normalize(u + 1, 1, k + 1)
                    high(u + 1, k, False)
                for o in range(KT):
                    if layer == 0 and not first:
                        act.wait_ge(turned_out, BASE + KT * (CHUNKS * n - 1) + o + 1)
                        squash(u, n, layer, 0, o, False, first=True)
                    elif layer == 1:
                        act.wait_ge(added, KT * (u - 1) + o + 1)
                        squash(u, n, layer, 0, o, False, first=True)
                    else:
                        squash(u, n, layer, 0, o, False, first=True)

            def layer0_rest(n):
                middle(n, 0)
                u, stage = UNITS * n + LAST, LAYERS * n + 1
                high(u, KT - 1, False)
                squash(u, n, 0, LAST, 0, True)
                squash(u, n, 0, LAST, 1, True)
                normalize_first(u + 1, stage, 0)
                squash(u, n, 0, LAST, 2, True)
                high(u + 1, 0, True)
                normalize_first(u + 1, stage, 1)
                high(u + 1, 1, True)
                squash(u, n, 0, LAST, 3, True)
                normalize_first(u + 1, stage, 2)
                high(u + 1, 2, True)
                normalize_first(u + 1, stage, 3)

            def layer1(n, incoming):
                first_unit(UNITS * n + CHUNKS, n, 1)
                middle(n, 1)
                u, stage = UNITS * n + CHUNKS + LAST, LAYERS * (n + 1)
                high(u, KT - 1, False)
                if not incoming:
                    for o in range(KT):
                        squash(u, n, 1, LAST, o, True)
                    return
                squash(u, n, 1, LAST, 0, True)
                squash(u, n, 1, LAST, 1, True)
                squash(u, n, 1, LAST, 2, True)
                normalize_first(u + 1, stage, 0)
                high(u + 1, 0, True)
                squash(u, n, 1, LAST, 3, True)
                normalize_first(u + 1, stage, 1)
                high(u + 1, 1, True)
                normalize_first(u + 1, stage, 2)
                high(u + 1, 2, True)
                normalize_first(u + 1, stage, 3)

            act.wait_ge(bias_come, 16 * LAYERS * QUADS)
            for l in range(LAYERS):
                act.wait_ge(w_come[l], 16 * QUADS)
                for q in range(QUADS):
                    raw, hi, _ = w_parts(l, q)
                    act.activation(hi, raw, ACT.Copy).then_inc(w_high, 1)
            normalize_first(0, 0, 0, first=True)
            for k in range(KT - 1):
                normalize_first(0, 0, k + 1, first=(k == 0))
                high(0, k, True, first=True)
            first_unit(0, 0, 0, first=True)
            with act.Fori(0, IMAGES - 1) as n:
                layer0_rest(n)
                layer1(n, True)
                first_unit(UNITS * (n + 1), n + 1, 0)
            layer0_rest(IMAGES - 1)
            layer1(IMAGES - 1, False)

        @block.vector
        def _(dve):
            def low(u, k):
                dve.wait_ge(hi_ready, KT * u + k + 1)
                dve.tensor_tensor(x_lo[:, k], xn[:, k % 2], x_hi[:, k].bitcast(F32), ALU.subtract)\
                    .then_inc(lo_ready, 1)

            def add(u, chunk, o):
                dve.wait_ge(tanh_done, KT * u + o + 1)
                dve.tensor_tensor(ring[:, chunk, o], ring[:, chunk, o], th[:, o], ALU.add).then_inc(added, 1)

            def turn_out(u, n, chunk, half, o):
                dve.wait_ge(added, KT * u + o + 1)
                if o == 0:
                    dve.wait_ge(stored[half], BASE + 8 * QUADS * (CHUNKS * n + chunk - half))
                dve.transpose(rows_out[:, half, :, o, :], th[:, o].rearrange("p (b i) -> p b i", i=Q))\
                    .then_inc(turned_out, 1)

            def stats_of_sum(u, chunk, o):
                dve.wait_ge(added, KT * u + o + 1)
                dve.bn_stats(stats[:, o, bass.ds(chunk * BN, BN)], ring[:, chunk, o])

            def turn_in(n, chunk, half, k, first=False):
                if k == 0:
                    dve.wait_ge(rows_come[half], 8 * QUADS * (CHUNKS * n + chunk - half) + 16 * QUADS)
                if not first:
                    dve.wait_ge(added, KT * (UNITS * (n - 1) + CHUNKS + chunk) + k + 1)
                dve.transpose(ring[:, chunk, k].rearrange("p (b i) -> p b i", i=Q), rows_in[:, half, :, k, :])\
                    .then_inc(turned_in, 1)

            def stats_of_input(n, chunk, k):
                dve.wait_ge(turned_in, KT * (CHUNKS * n + chunk) + k + 1)
                dve.bn_stats(stats[:, k, bass.ds(chunk * BN, BN)], ring[:, chunk, k])

            def aggregate(stage, k):
                dve.drain()
                dve.bn_aggr(agg[:, k], stats[:, k]).then_inc(agg_ready, 1)

            def group_mean_and_spread(stage, k):
                dve.wait_ge(mean_done, KT * stage + k + 1)
                dve.tensor_scalar(minus_mean[:, k:k + 1], small[:, k:k + 1], -1.0, None, ALU.mult)\
                    .then_inc(mean_kept, 1)
                dve.wait_ge(mean_kept, KT * stage + k + 1)
                dve.tensor_tensor(diff[:, k:k + 1], agg[:, k, 0:1], minus_mean[:, k:k + 1], ALU.add)\
                    .then_inc(diff_ready, 1)
                dve.wait_ge(diff_ready, KT * stage + k + 1)
                dve.scalar_tensor_tensor(spread[:, k:k + 1], diff[:, k:k + 1], diff[:, k:k + 1],
                                         agg[:, k, 1:2], ALU.mult, ALU.add).then_inc(spread_ready, 1)

            def group_variance(stage, k):
                dve.wait_ge(spread_done, KT * stage + k + 1)
                dve.tensor_scalar(var_eps[:, k:k + 1], small[:, KT + k:KT + k + 1], EPS, None, ALU.add)\
                    .then_inc(var_ready, 1)

            def finish_layer0(u, chunk):
                add(u - 1, chunk - 1, 0)
                add(u - 1, chunk - 1, 1)
                stats_of_sum(u - 1, chunk - 1, 0)
                add(u - 1, chunk - 1, 2)
                low(u, KT - 1)
                add(u - 1, chunk - 1, 3)

            def first_unit(u):
                low(u, KT - 1)
                for k in range(KT - 1):
                    low(u + 1, k)

            def layer0_rest(n):
                with dve.Fori(0, CHUNKS // 2 - 1) as pair:
                    for h in range(2):
                        c = 2 * pair + h + 1
                        u = UNITS * n + c
                        finish_layer0(u, c)
                        for k in range(KT - 1):
                            stats_of_sum(u - 1, c - 1, k + 1)
                        for k in range(KT - 1):
                            low(u + 1, k)
                u, stage = UNITS * n + LAST, LAYERS * n + 1
                finish_layer0(u, LAST)
                add(u, LAST, 0)
                stats_of_sum(u - 1, LAST - 1, 1)
                stats_of_sum(u, LAST, 0)
                aggregate(stage, 0)
                stats_of_sum(u - 1, LAST - 1, 2)
                group_mean_and_spread(stage, 0)
                stats_of_sum(u - 1, LAST - 1, 3)
                group_variance(stage, 0)
                add(u, LAST, 1)
                stats_of_sum(u, LAST, 1)
                aggregate(stage, 1)
                group_mean_and_spread(stage, 1)
                group_variance(stage, 1)
                add(u, LAST, 2)
                stats_of_sum(u, LAST, 2)
                low(u + 1, 0)
                aggregate(stage, 2)
                low(u + 1, 1)
                group_mean_and_spread(stage, 2)
                group_variance(stage, 2)
                add(u, LAST, 3)
                stats_of_sum(u, LAST, 3)
                aggregate(stage, 3)
                group_mean_and_spread(stage, 3)
                group_variance(stage, 3)
                low(u + 1, 2)

            def layer1(n, incoming):
                first_unit(UNITS * n + CHUNKS)
                for c in range(1, LAST):
                    u, h = UNITS * n + CHUNKS + c, (c - 1) % 2
                    turn_out(u - 1, n, c - 1, h, 0)
                    low(u, KT - 1)
                    if incoming:
                        turn_in(n + 1, c - 1, h, 0)
                    turn_out(u - 1, n, c - 1, h, 1)
                    if incoming:
                        turn_in(n + 1, c - 1, h, 1)
                        stats_of_input(n + 1, c - 1, 0)
                    low(u + 1, 0)
                    turn_out(u - 1, n, c - 1, h, 2)
                    if incoming:
                        turn_in(n + 1, c - 1, h, 2)
                        stats_of_input(n + 1, c - 1, 1)
                    low(u + 1, 1)
                    turn_out(u - 1, n, c - 1, h, 3)
                    if incoming:
                        turn_in(n + 1, c - 1, h, 3)
                        stats_of_input(n + 1, c - 1, 2)
                    low(u + 1, 2)
                    if incoming:
                        stats_of_input(n + 1, c - 1, 3)
                u, stage = UNITS * n + CHUNKS + LAST, LAYERS * (n + 1)
                turn_out(u - 1, n, LAST - 1, 0, 0)
                low(u, KT - 1)
                if not incoming:
                    for o in range(1, KT):
                        turn_out(u - 1, n, LAST - 1, 0, o)
                    for o in range(KT):
                        turn_out(u, n, LAST, 1, o)
                    return
                turn_in(n + 1, LAST - 1, 0, 0)
                turn_out(u - 1, n, LAST - 1, 0, 1)
                stats_of_input(n + 1, LAST - 1, 0)
                turn_in(n + 1, LAST - 1, 0, 1)
                turn_out(u - 1, n, LAST - 1, 0, 2)
                turn_in(n + 1, LAST - 1, 0, 2)
                turn_out(u - 1, n, LAST - 1, 0, 3)
                turn_in(n + 1, LAST - 1, 0, 3)
                turn_in(n + 1, LAST, 1, 0)
                stats_of_input(n + 1, LAST - 1, 1)
                stats_of_input(n + 1, LAST, 0)
                aggregate(stage, 0)
                stats_of_input(n + 1, LAST - 1, 2)
                group_mean_and_spread(stage, 0)
                turn_out(u, n, LAST, 1, 0)
                group_variance(stage, 0)
                turn_in(n + 1, LAST, 1, 1)
                stats_of_input(n + 1, LAST - 1, 3)
                stats_of_input(n + 1, LAST, 1)
                aggregate(stage, 1)
                turn_out(u, n, LAST, 1, 1)
                group_mean_and_spread(stage, 1)
                turn_in(n + 1, LAST, 1, 2)
                group_variance(stage, 1)
                low(u + 1, 0)
                turn_out(u, n, LAST, 1, 2)
                stats_of_input(n + 1, LAST, 2)
                aggregate(stage, 2)
                low(u + 1, 1)
                group_mean_and_spread(stage, 2)
                group_variance(stage, 2)
                turn_in(n + 1, LAST, 1, 3)
                turn_out(u, n, LAST, 1, 3)
                stats_of_input(n + 1, LAST, 3)
                aggregate(stage, 3)
                group_mean_and_spread(stage, 3)
                group_variance(stage, 3)
                low(u + 1, 2)

            dve.sem_inc(turned_out, BASE)
            for c in range(CHUNKS):
                turn_in(0, c, c % 2, 0, first=True)
                for k in range(1, KT):
                    turn_in(0, c, c % 2, k, first=True)
                    stats_of_input(0, c, k - 1)
                stats_of_input(0, c, KT - 1)
            for k in range(KT):
                aggregate(0, k)
                group_mean_and_spread(0, k)
                group_variance(0, k)
            for k in range(KT - 1):
                low(0, k)
            first_unit(0)
            with dve.Fori(0, IMAGES - 1) as n:
                layer0_rest(n)
                layer1(n, True)
                first_unit(UNITS * (n + 1))
            layer0_rest(IMAGES - 1)
            layer1(IMAGES - 1, False)


def kernel(**inputs):
    import numpy as _np
    import concourse.bacc as _bacc
    from concourse import mybir as _mybir
    from concourse.bass_utils import run_bass_kernel_spmd as _run

    nc = _bacc.Bacc("TRN2", target_bir_lowering=False, num_devices=1, dynamic_dma_scratch_size=1024)
    arrays, args = {}, []
    for name in ("x", "L0_conv_W", "L0_conv_b", "L1_conv_W", "L1_conv_b"):
        a = _np.ascontiguousarray(inputs[name])
        arrays[f"in_{name}"] = a
        args.append(nc.dram_tensor(f"in_{name}", a.shape, _mybir.dt.from_np(a.dtype), kind="ExternalInput").ap())
    shape = (IMAGES, HEIGHT, WIDTH, CHANNELS)
    args.append(nc.dram_tensor("out", shape, _mybir.dt.float32, kind="ExternalOutput").ap())
    preact_conv_stack(nc, *args)
    result = _run(nc, [arrays], core_ids=[0])
    return result.results[0]["out"]
```

```python
from contextlib import ExitStack

import concourse.bass as bass
from concourse import mybir

F32 = mybir.dt.float32
F32R = mybir.dt.float32r
ALU = mybir.AluOpType
ACT = mybir.ActivationFunctionType

P = 128
IMAGES, HEIGHT, WIDTH, CHANNELS = 8, 64, 128, 512
GROUPS = 32
PER_GROUP = CHANNELS // GROUPS
EPS = 1e-5
LAYERS = 2

TOKENS = HEIGHT * WIDTH
KT = CHANNELS // P
CHUNK = 512
CHUNKS = TOKENS // CHUNK
UNITS = LAYERS * CHUNKS
LAST = CHUNKS - 1
STEPS = KT * KT
Q = 32
QUADS = P // Q
BLOCKS = CHUNK // Q
AT_EARLY = 3
AT_L1 = (8, 12, 17, 22)
AT_IN = (7, 12, 17, 21)
THREES = CHUNKS // 3
FIRST_TURNED = KT * (THREES + 1)
BN = 6
EARLY = CHUNKS - 2
BASE = 1


def preact_conv_stack(nc, x, w0, b0, w1, b1, out):
    def quads(a):
        return a.rearrange("n h w c -> n (h w) c").rearrange("n (j b i) (q d) -> n j q i b d", b=BLOCKS, i=Q, q=QUADS)

    x_quads, out_quads = quads(x), quads(out)
    x_tokens = x[0].rearrange("h w c -> (h w) c").rearrange("(j g p) c -> j p g c", g=KT, p=P)

    with ExitStack() as ctx:
        def sb(name, shape, dt=F32):
            return ctx.enter_context(nc.sbuf_tensor(name, shape, dt))

        def psum(name, shape):
            return ctx.enter_context(nc.psum_tensor(name, shape, F32))

        def sem(name):
            return ctx.enter_context(nc.semaphore(name))

        ring = sb("ring", [P, CHUNKS, KT, CHUNK])
        w_hi = sb("w_hi", [P, LAYERS, KT, CHANNELS], F32R)
        w_lo = sb("w_lo", [P, LAYERS, KT, CHANNELS], F32R)
        x_hi = sb("x_hi", [P, KT, CHUNK], F32R)
        x_lo = sb("x_lo", [P, KT, CHUNK], F32R)
        xn = sb("xn", [P, 2, CHUNK])
        th = sb("th", [P, KT, CHUNK])
        rows_in = sb("rows_in", [P, 2, BLOCKS, KT, Q])
        rows_out = sb("rows_out", [P, 2, BLOCKS, KT, Q])
        bias = sb("bias", [P, LAYERS, KT])
        group_mean = sb("group_mean", [P, P])
        stats = sb("stats", [P, KT, (CHUNKS + 1) * BN])
        early_agg = sb("early_agg", [P, KT, 2])
        minus_early = sb("minus_early", [P, KT])
        agg = sb("agg", [P, KT, 2])
        channel_var = sb("channel_var", [P, KT])
        moments = sb("moments", [P, KT, 2])
        minus_drift = sb("minus_drift", [P, KT])
        minus_mean = sb("minus_mean", [P, KT])
        var_eps = sb("var_eps", [P, KT])
        power = sb("power", [P, 1])
        rstd = sb("rstd", [P, KT])
        shift = sb("shift", [P, KT])

        scratch = rows_out[:, 0].rearrange("p b k i -> p (b k i)").rearrange("p (k c) -> p k c", k=KT)
        tile_rows = [a.rearrange("p (g c) -> p g c", g=KT)
                     for a in (rows_out[:, 1].rearrange("p b k i -> p (b k i)"),
                               ring[:, LAST].rearrange("p k t -> p (k t)"))]
        identity = xn[:, 0, 0:P]
        w_raw = [th[:, :, :], scratch]

        acc = [[psum(f"acc{h}{o}", [P, CHUNK]) for o in range(KT)] for h in range(2)]
        early_sums = acc[0][KT - 1]
        moment_sums = acc[1][0]

        filled = sem("filled")
        identity_ready = sem("identity_ready")
        consts = sem("consts")
        w_come = [sem(f"w_come{l}") for l in range(LAYERS)]
        bias_come = sem("bias_come")
        w_high = sem("w_high")
        w_split = sem("w_split")
        rows_come = [sem(f"rows_come{i}") for i in range(2)]
        stored = [sem(f"stored{i}") for i in range(2)]
        dve_rows_come = [sem(f"dve_rows_come{i}") for i in range(2)]
        pe_rows_come = [sem(f"pe_rows_come{i}") for i in range(4)]
        reordered = sem("reordered")
        transposed = sem("transposed")
        copied_in = sem("copied_in")
        turned_in = sem("turned_in")
        staged = sem("staged")
        turned_out = sem("turned_out")
        xn_ready = sem("xn_ready")
        hi_ready = sem("hi_ready")
        lo_ready = sem("lo_ready")
        steps_done = sem("steps_done")
        tanh_done = sem("tanh_done")
        added = sem("added")
        agg_ready = sem("agg_ready")
        parts_ready = sem("parts_ready")
        moments_ready = sem("moments_ready")
        moments_done = sem("moments_done")
        drift_kept = sem("drift_kept")
        var_ready = sem("var_ready")
        mean_ready = sem("mean_ready")
        early_ready = sem("early_ready")
        early_done = sem("early_done")
        early_kept = sem("early_kept")
        rstd_ready = sem("rstd_ready")
        shift_ready = sem("shift_ready")

        def used(u, k, by_output):
            return STEPS * u + ((KT - 1) * KT + k + 1 if by_output else KT * (k + 1))

        def summed(u, o, by_output):
            return STEPS * u + (KT * (o + 1) if by_output else (KT - 1) * KT + o + 1)

        def tanhs(u, o):
            return KT * (u + 1) + o + 1

        def loads(n, c):
            return CHUNKS // 2 * (n - 1) + c // 2 + 1 + (n if c % 2 == 0 else 0)

        def turns(n, c, k):
            return FIRST_TURNED + KT * (CHUNKS * (n - 1) + c) + k + 1

        def copies(m, k):
            return KT * (m + 2) + k + 1

        def pe_chunk(m):
            return 3 * (m // 2) + 1 + m % 2

        def w_parts(l, q):
            raw = w_raw[l].rearrange("p k (q o i) -> p q k o i", q=QUADS, i=Q)[:, q]
            hi, lo = (w[:, l].rearrange("p k (o q i) -> p q k o i", q=QUADS, i=Q)[:, q] for w in (w_hi, w_lo))
            return raw, hi, lo

        block = ctx.enter_context(nc.Block())

        @block.sync
        def _(sp):
            def load_half(n, c, half):
                for q in range(QUADS):
                    sp.dma_start(rows_in[Q * q:Q * q + Q, half].rearrange("i b k d -> i b (k d)"),
                                 x_quads[n, c, q]).then_inc(rows_come[half], 16)

            def load(n, c, half):
                sp.wait_ge(turned_in, turns(n, c - 2, KT - 1))
                load_half(n, c, half)

            def load_for_dve(j):
                if j > 1:
                    sp.wait_ge(turned_in, KT * (j - 1))
                for q in range(QUADS):
                    sp.dma_start(rows_in[Q * q:Q * q + Q, j % 2].rearrange("i b k d -> i b (k d)"),
                                 x_quads[0, 3 * j, q]).then_inc(dve_rows_come[j % 2], 16)

            def load_for_pe(m):
                if m > 3:
                    sp.wait_ge(reordered, KT * (m - 3))
                c = pe_chunk(m)
                sp.dma_start(ring[:, c], x_tokens[c]).then_inc(pe_rows_come[m % 4], 16)

            def load_w(l, w, b):
                w_quads = w.rearrange("(q k i) o -> q i k o", q=QUADS, i=Q)
                b_quads = b.rearrange("(q k i) -> q i k", q=QUADS, i=Q)
                for q in range(QUADS):
                    sp.dma_start(w_raw[l][Q * q:Q * q + Q], w_quads[q]).then_inc(w_come[l], 16)
                    with nc.allow_non_contiguous_dma(reason="one bias value per partition"):
                        sp.dma_start(bias[Q * q:Q * q + Q, l, :], b_quads[q]).then_inc(bias_come, 16)

            def store(n, c, half):
                sp.wait_ge(turned_out, BASE + KT * (CHUNKS * n + c + 1))
                for q in range(QUADS):
                    sp.dma_start(out_quads[n, c, q], rows_out[Q * q:Q * q + Q, half]
                                 .rearrange("i b k d -> i b (k d)")).then_inc(stored[half], 16)

            def load_last_early(n, first=False):
                sp.wait_ge(turned_in, FIRST_TURNED if first else turns(n - 1, LAST - 1, KT - 1))
                load_half(n, LAST, 0)

            def exchange(n, more=True):
                sp.wait_ge(staged, KT * (n + 1))
                load_half(n + 1, 0, 0)
                load(n + 1, 1, 1)
                with sp.Fori(0, CHUNKS // 2 - 1) as pair:
                    for h in range(2):
                        store(n, 2 * pair + h, h)
                        load(n + 1, 2 * pair + h + 2, h)
                store(n, LAST - 1, 0)
                if more:
                    load_last_early(n + 2)
                store(n, LAST, 1)

            for h in range(2):
                sp.sem_inc(stored[h], BASE)
            load_for_dve(0)
            for j in range(THREES):
                load_for_pe(2 * j)
                load_for_dve(j + 1)
                load_for_pe(2 * j + 1)
                if j == 1:
                    load_w(0, w0, b0)
            load_w(1, w1, b1)
            load_last_early(1, first=True)
            with sp.Fori(0, IMAGES - 2) as n:
                exchange(n)
            exchange(IMAGES - 2, False)
            with sp.Fori(0, CHUNKS // 2) as pair:
                for h in range(2):
                    store(IMAGES - 1, 2 * pair + h, h)
            for h in range(2):
                sp.wait_ge(stored[h], BASE + 16 * QUADS * IMAGES * CHUNKS // 2)

        @block.gpsimd
        def _(pool):
            pool.memset(identity, 1.0).then_inc(filled, 1)
            pool.memset(group_mean[:, :], 1.0 / PER_GROUP).then_inc(filled, 1)
            pool.memset(power[:, :], -0.5).then_inc(consts, 1)
            pool.wait_ge(filled, 1)
            pool.affine_select(out=identity, in_=identity, compare_op=ALU.is_equal, fill=0.0, base=0,
                               pattern=[[-1, P]], channel_multiplier=1).then_inc(identity_ready, 1)
            pool.wait_ge(filled, 2)
            blocks = group_mean[:, :].rearrange("p (g i) -> p g i", i=PER_GROUP)
            pool.affine_select(out=blocks, in_=blocks, compare_op=ALU.is_ge, fill=0.0, base=0,
                               pattern=[[-PER_GROUP, P // PER_GROUP], [0, PER_GROUP]],
                               channel_multiplier=1).then_inc(filled, 1)
            pool.wait_ge(filled, 3)
            pool.affine_select(out=blocks, in_=blocks, compare_op=ALU.is_ge, fill=0.0, base=PER_GROUP - 1,
                               pattern=[[PER_GROUP, P // PER_GROUP], [0, PER_GROUP]],
                               channel_multiplier=-1).then_inc(consts, 1)
            pool.wait_ge(consts, 1)

            def split_w(l):
                for q in range(QUADS):
                    raw, hi, lo = w_parts(l, q)
                    pool.wait_ge(w_high, QUADS * l + q + 1)
                    pool.tensor_tensor(lo, raw, hi.bitcast(F32), ALU.subtract).then_inc(w_split, 1)

            def scale_and_shift(stage, k):
                pool.wait_ge(var_ready, KT * stage + k + 1)
                pool.tensor_tensor(rstd[:, k:k + 1], var_eps[:, k:k + 1], power[:, :], ALU.pow)\
                    .then_inc(rstd_ready, 1)
                pool.wait_ge(rstd_ready, KT * stage + k + 1)
                pool.wait_ge(mean_ready, KT * stage + k + 1)
                pool.tensor_tensor(shift[:, k:k + 1], minus_mean[:, k:k + 1], rstd[:, k:k + 1], ALU.mult)\
                    .then_inc(shift_ready, 1)

            def add(u, chunk, o):
                pool.wait_ge(tanh_done, tanhs(u, o))
                pool.tensor_tensor(th[:, o], ring[:, chunk, o], th[:, o], ALU.add).then_inc(added, 1)

            def image(n, more):
                for k in range(KT):
                    scale_and_shift(LAYERS * n + 1, k)
                u = UNITS * n + CHUNKS
                with pool.Fori(0, LAST) as c:
                    for o in range(KT):
                        add(u + c, c, o)
                for o in range(KT):
                    if more and o == KT - 1:
                        scale_and_shift(LAYERS * (n + 1), o)
                    add(u + LAST, LAST, o)
                    if more and o < KT - 1:
                        scale_and_shift(LAYERS * (n + 1), o)

            split_w(0)
            for k in range(KT):
                scale_and_shift(0, k)
            split_w(1)
            with pool.Fori(0, IMAGES - 1) as n:
                image(n, True)
            image(IMAGES - 1, False)

        @block.tensor
        def _(pe):
            def step(u, layer, by_output, h, s, first=False):
                o, k = divmod(s, KT) if by_output else (s % KT, s // KT)
                bank = acc[h][o][:, :]
                if o == 0:
                    pe.wait_ge(lo_ready, KT * u + k + 1)
                if k == 0 and not first:
                    pe.wait_ge(tanh_done, tanhs(u - 2, o))
                cols = slice(o * P, (o + 1) * P)
                pe.matmul(bank, w_lo[:, layer, k, cols], x_hi[:, k], start=(k == 0), stop=False)
                pe.matmul(bank, w_hi[:, layer, k, cols], x_lo[:, k], start=False, stop=False)
                pe.matmul(bank, w_hi[:, layer, k, cols], x_hi[:, k], start=False,
                          stop=(k == KT - 1)).then_inc(steps_done, 1)

            def early_means(stage, last=None):
                pe.wait_ge(early_ready, KT * stage + KT)
                if last is not None:
                    pe.wait_ge(tanh_done, tanhs(last - 1, KT - 1))
                pe.matmul(early_sums[:, 0:KT], group_mean[:, :], early_agg[:, :, 0], start=True, stop=True)\
                    .then_inc(early_done, 1)

            def group_moments(stage, k, last=None):
                pe.wait_ge(moments_ready, KT * stage + k + 1)
                if k:
                    pe.wait_ge(var_ready, KT * stage + k)
                elif last is not None:
                    pe.wait_ge(tanh_done, tanhs(last, 0))
                pe.matmul(moment_sums[:, 2 * k:2 * k + 2], group_mean[:, :], moments[:, k], start=True, stop=True)\
                    .then_inc(moments_done, 1)

            def unit(u, layer, by_output, h, between, first=False):
                for s in range(STEPS):
                    step(u, layer, by_output, h, s, first)
                    for what, *args in between.get(s, ()):
                        what(*args)

            def middle(n, layer):
                with pe.Fori(0, CHUNKS // 2 - 1) as pair:
                    for i in range(2):
                        j = 2 * pair + i + 1
                        unit(UNITS * n + CHUNKS * layer + j, layer, False, 1 - i, {})

            def layer0_first(n, first=False):
                stage = LAYERS * n
                if first:
                    between = {2: [(group_moments, 0, 2)], 6: [(group_moments, 0, 3)]}
                else:
                    between = {AT_IN[2] - STEPS: [(group_moments, stage, 2)], AT_IN[3] - STEPS: [(group_moments, stage, 3)]}
                unit(UNITS * n, 0, False, 0, between, first)

            def layer0_rest(n):
                middle(n, 0)
                stage = LAYERS * n + 1
                u = UNITS * n + LAST
                unit(u, 0, True, 1,
                     {AT_EARLY: [(early_means, stage, u)], AT_L1[0]: [(group_moments, stage, 0, u)],
                      AT_L1[1]: [(group_moments, stage, 1)]})

            def layer1(n, incoming):
                stage = LAYERS * n + 1
                unit(UNITS * n + CHUNKS, 1, False, 0,
                     {AT_L1[2] - STEPS: [(group_moments, stage, 2)], AT_L1[3] - STEPS: [(group_moments, stage, 3)]})
                middle(n, 1)
                u = UNITS * n + CHUNKS + LAST
                between = {}
                if incoming:
                    stage = LAYERS * (n + 1)
                    between = {AT_EARLY: [(early_means, stage, u)], AT_IN[0]: [(group_moments, stage, 0, u)],
                               AT_IN[1]: [(group_moments, stage, 1)]}
                unit(u, 1, True, 1, between)

            def transpose_chunk(m, i):
                pe.wait_ge(reordered, KT * (m + 1))
                for k in range(KT):
                    pe.wait_ge(copied_in, copies(m - 2, k))
                    for g in range(KT):
                        done = pe.transpose(acc[i][k][:, P * g:P * g + P], tile_rows[i][:, g, P * k:P * k + P],
                                            identity)
                    done.then_inc(transposed, 1)

            pe.wait_ge(identity_ready, 1)
            with pe.Fori(0, THREES) as j:
                for i in range(2):
                    transpose_chunk(2 * j + i, i)
            pe.wait_ge(copied_in, copies(2 * THREES - 1, KT - 1))
            pe.wait_ge(consts, 2)
            early_means(0)
            group_moments(0, 0)
            group_moments(0, 1)
            pe.wait_ge(w_split, QUADS)
            layer0_first(0, first=True)
            with pe.Fori(0, IMAGES - 1) as n:
                layer0_rest(n)
                layer1(n, True)
                layer0_first(n + 1)
            layer0_rest(IMAGES - 1)
            layer1(IMAGES - 1, False)

        @block.scalar
        def _(act):
            def normalize(u, chunk, k, first=False):
                if not first:
                    act.wait_ge(lo_ready, KT * u + k - 1)
                act.activation(xn[:, k % 2], ring[:, chunk, k], ACT.Identity, bias=shift[:, k:k + 1],
                               scale=rstd[:, k:k + 1]).then_inc(xn_ready, 1)

            def normalize_first(u, stage, k, first=False):
                act.wait_ge(shift_ready, KT * stage + k + 1)
                normalize(u, 0, k, first)

            def high(u, k, by_output, first=False):
                act.wait_ge(xn_ready, KT * u + k + 1)
                if not first:
                    act.wait_ge(steps_done, used(u - 1, k, by_output))
                act.activation(x_hi[:, k], xn[:, k % 2], ACT.Copy).then_inc(hi_ready, 1)

            def squash(u, n, layer, chunk, h, o, by_output, behind):
                act.wait_ge(steps_done, summed(u, o, by_output))
                if behind == 0:
                    act.wait_ge(added, KT * (u - 1) + o + 1)
                elif behind == 1:
                    act.wait_ge(turned_out, BASE + KT * (CHUNKS * n + chunk - 1) + o + 1)
                act.activation(th[:, o], acc[h][o][:, :], ACT.Tanh, bias=bias[:, layer, o:o + 1])\
                    .then_inc(tanh_done, 1)

            def prepare(u, chunk):
                normalize(u, chunk, 0)
                normalize(u, chunk, 1)
                high(u, 0, False)
                high(u, 1, False)
                normalize(u, chunk, 2)
                high(u, 2, False)

            def squash_all(u, n, layer, chunk, next_chunk, h, behind):
                for o in range(KT):
                    if o == 1:
                        normalize(u + 1, next_chunk, KT - 1)
                    if o == 2:
                        high(u + 1, KT - 1, False)
                    squash(u, n, layer, chunk, h, o, False, behind)

            def middle(n, layer):
                with act.Fori(0, CHUNKS // 2 - 1) as pair:
                    for i in range(2):
                        c = 2 * pair + i + 1
                        u = UNITS * n + CHUNKS * layer + c
                        prepare(u + 1, c + 1)
                        squash_all(u, n, layer, c, c + 1, 1 - i, layer)

            def first_unit(u, n, layer, first=False):
                high(u, KT - 1, True, first)
                if layer == 0 and not first:
                    squash(u - 1, n - 1, 1, LAST, 1, KT - 1, True, 1)
                prepare(u + 1, 1)
                squash_all(u, n, layer, 0, 1, 0, None if first else 1 - layer)

            def layer0_rest(n):
                middle(n, 0)
                u, stage = UNITS * n + LAST, LAYERS * n + 1
                squash(u, n, 0, LAST, 1, 0, True, 0)
                squash(u, n, 0, LAST, 1, 1, True, 0)
                normalize_first(u + 1, stage, 0)
                squash(u, n, 0, LAST, 1, 2, True, 0)
                high(u + 1, 0, True)
                normalize_first(u + 1, stage, 1)
                squash(u, n, 0, LAST, 1, 3, True, 0)
                high(u + 1, 1, True)
                normalize_first(u + 1, stage, 2)
                high(u + 1, 2, True)
                normalize_first(u + 1, stage, 3)

            def layer1(n, incoming):
                first_unit(UNITS * n + CHUNKS, n, 1)
                middle(n, 1)
                u, stage = UNITS * n + CHUNKS + LAST, LAYERS * (n + 1)
                if not incoming:
                    for o in range(KT):
                        squash(u, n, 1, LAST, 1, o, True, 1)
                    return
                squash(u, n, 1, LAST, 1, 0, True, 1)
                squash(u, n, 1, LAST, 1, 1, True, 1)
                normalize_first(u + 1, stage, 0)
                high(u + 1, 0, True)
                squash(u, n, 1, LAST, 1, 2, True, 1)
                normalize_first(u + 1, stage, 1)
                high(u + 1, 1, True)
                normalize_first(u + 1, stage, 2)
                high(u + 1, 2, True)
                normalize_first(u + 1, stage, 3)

            def reorder(m):
                act.wait_ge(pe_rows_come[m % 4], 16 * (m // 4 + 1))
                rows = ring[:, pe_chunk(m)]
                for g in range(KT):
                    act.activation(tile_rows[m % 2][:, g].rearrange("p (k q d) -> p k q d", k=KT, q=QUADS),
                                   rows[:, g].rearrange("p (q k d) -> p k q d", k=KT, q=QUADS),
                                   ACT.Copy).then_inc(reordered, 1)

            def copy_in(m):
                for k in range(KT):
                    act.wait_ge(transposed, KT * m + k + 1)
                    act.activation(ring[:, pe_chunk(m), k], acc[m % 2][k][:, :], ACT.Copy).then_inc(copied_in, 1)

            def round_w(l, q):
                raw, hi, _ = w_parts(l, q)
                act.activation(hi, raw, ACT.Copy).then_inc(w_high, 1)

            act.sem_inc(tanh_done, KT)
            act.sem_inc(copied_in, 2 * KT)
            reorder(0)
            for m in range(4):
                reorder(m + 1)
                copy_in(m)
            act.wait_ge(w_come[0], 16 * QUADS)
            for q in range(QUADS):
                round_w(0, q)
            for m in range(4, 2 * THREES):
                if m + 1 < 2 * THREES:
                    reorder(m + 1)
                copy_in(m)
            act.wait_ge(bias_come, 16 * LAYERS * QUADS)
            act.wait_ge(w_come[1], 16 * QUADS)
            for k in range(KT):
                normalize_first(0, 0, k, first=(k < 2))
                if k < KT - 1:
                    high(0, k, True, first=True)
                round_w(1, k)
            first_unit(0, 0, 0, first=True)
            with act.Fori(0, IMAGES - 1) as n:
                layer0_rest(n)
                layer1(n, True)
                first_unit(UNITS * (n + 1), n + 1, 0)
            layer0_rest(IMAGES - 1)
            layer1(IMAGES - 1, False)

        @block.vector
        def _(dve):
            def low(u, k):
                dve.wait_ge(hi_ready, KT * u + k + 1)
                dve.tensor_tensor(x_lo[:, k], xn[:, k % 2], x_hi[:, k].bitcast(F32), ALU.subtract)\
                    .then_inc(lo_ready, 1)

            def add(u, chunk, o):
                dve.wait_ge(tanh_done, tanhs(u, o))
                dve.tensor_tensor(ring[:, chunk, o], ring[:, chunk, o], th[:, o], ALU.add).then_inc(added, 1)

            def turn_out(u, n, chunk, half, o):
                dve.wait_ge(added, KT * u + o + 1)
                if o == 0:
                    dve.wait_ge(stored[half], BASE + 8 * QUADS * (CHUNKS * n + chunk - half))
                dve.transpose(rows_out[:, half, :, o, :], th[:, o].rearrange("p (b i) -> p b i", i=Q))\
                    .then_inc(turned_out, 1)

            def stats_of_sum(u, chunk, o):
                dve.wait_ge(added, KT * u + o + 1)
                dve.bn_stats(stats[:, o, bass.ds(chunk * BN, BN)], ring[:, chunk, o])

            def turn_in(n, chunk, half, k):
                if k == 0:
                    dve.wait_ge(rows_come[half], 16 * QUADS * loads(n, chunk))
                dve.wait_ge(added, KT * (UNITS * (n - 1) + CHUNKS + chunk) + k + 1)
                dve.transpose(ring[:, chunk, k].rearrange("p (b i) -> p b i", i=Q), rows_in[:, half, :, k, :])\
                    .then_inc(turned_in, 1)

            def stats_of_input(n, chunk, k):
                dve.wait_ge(turned_in, turns(n, chunk, k))
                dve.bn_stats(stats[:, k, bass.ds((chunk + 1) * BN, BN)], ring[:, chunk, k])

            def first_turn_in(chunk):
                j = chunk // 3
                dve.wait_ge(dve_rows_come[j % 2], 16 * QUADS * (j // 2 + 1))
                if chunk == LAST:
                    dve.wait_ge(transposed, KT * 2 * THREES)
                dve.transpose(ring[:, chunk].rearrange("p k (b i) -> p k b i", i=Q),
                              rows_in[:, j % 2].rearrange("p b k i -> p k b i")).then_inc(turned_in, KT)

            def first_stats(chunk, k):
                j, i = divmod(chunk, 3)
                if i:
                    dve.wait_ge(copied_in, copies(2 * j + i - 1, k))
                else:
                    dve.wait_ge(turned_in, KT * j + k + 1)
                dve.bn_stats(stats[:, k, (chunk + 1) * BN:(chunk + 2) * BN], ring[:, chunk, k])

            def stage_last(n):
                dve.wait_ge(rows_come[0], 16 * QUADS * (loads(n, 0) - 1))
                dve.wait_ge(stored[0], BASE + 8 * QUADS * CHUNKS * (n - 1))
                for k in range(KT):
                    dve.transpose(scratch[:, k].rearrange("p (b i) -> p b i", i=Q), rows_in[:, 0, :, k, :])\
                        .then_inc(staged, 1)
                for k in range(KT):
                    dve.wait_ge(staged, KT * (n - 1) + k + 1)
                    dve.bn_stats(stats[:, k, CHUNKS * BN:(CHUNKS + 1) * BN], scratch[:, k])

            def aggregate_early(base):
                dve.drain()
                for k in range(KT):
                    dve.bn_aggr(early_agg[:, k], stats[:, k, base * BN:(base + EARLY) * BN]).then_inc(early_ready, 1)

            def keep_early(stage):
                dve.wait_ge(early_done, stage + 1)
                dve.tensor_scalar(minus_early[:, :], early_sums[:, 0:KT], -1.0, None, ALU.mult)\
                    .then_inc(early_kept, 1)

            def channel_moments(stage, k, base):
                dve.drain()
                dve.bn_aggr(agg[:, k], stats[:, k, base * BN:(base + CHUNKS) * BN]).then_inc(agg_ready, 1)
                if k == 0:
                    dve.wait_ge(early_kept, stage + 1)
                dve.wait_ge(agg_ready, KT * stage + k + 1)
                dve.tensor_tensor(moments[:, k, 0:1], agg[:, k, 0:1], minus_early[:, k:k + 1], ALU.add)\
                    .then_inc(parts_ready, 1)
                dve.tensor_scalar(channel_var[:, k:k + 1], agg[:, k, 1:2], EPS, None, ALU.add)\
                    .then_inc(parts_ready, 1)
                dve.wait_ge(parts_ready, 2 * (KT * stage + k + 1))
                dve.scalar_tensor_tensor(moments[:, k, 1:2], moments[:, k, 0:1], moments[:, k, 0:1],
                                         channel_var[:, k:k + 1], ALU.mult, ALU.add).then_inc(moments_ready, 1)

            def group_variance(stage, k):
                dve.wait_ge(moments_done, KT * stage + k + 1)
                dve.tensor_scalar(minus_drift[:, k:k + 1], moment_sums[:, 2 * k:2 * k + 1], -1.0, None, ALU.mult)\
                    .then_inc(drift_kept, 1)
                dve.wait_ge(drift_kept, KT * stage + k + 1)
                dve.scalar_tensor_tensor(var_eps[:, k:k + 1], minus_drift[:, k:k + 1], moment_sums[:, 2 * k:2 * k + 1],
                                         moment_sums[:, 2 * k + 1:2 * k + 2], ALU.mult, ALU.add).then_inc(var_ready, 1)
                dve.tensor_tensor(minus_mean[:, k:k + 1], minus_drift[:, k:k + 1], minus_early[:, k:k + 1], ALU.add)\
                    .then_inc(mean_ready, 1)

            def first_unit(u, n, layer, first=False):
                low(u, KT - 1)
                if layer == 0 and not first:
                    for o in range(KT):
                        turn_out(u - 1, n - 1, LAST, 1, o)
                        turn_in(n, LAST, 1, o)
                        if o:
                            low(u + 1, o - 1)
                else:
                    for k in range(KT - 1):
                        low(u + 1, k)

            def layer0_middle(n, begin, end):
                with dve.Fori(begin, end) as pair:
                    for i in range(2):
                        c = 2 * pair + i + 1
                        u = UNITS * n + c
                        add(u - 1, c - 1, 0)
                        add(u - 1, c - 1, 1)
                        low(u, KT - 1)
                        add(u - 1, c - 1, 2)
                        add(u - 1, c - 1, 3)
                        stats_of_sum(u - 1, c - 1, 0)
                        stats_of_sum(u - 1, c - 1, 1)
                        low(u + 1, 0)
                        stats_of_sum(u - 1, c - 1, 2)
                        stats_of_sum(u - 1, c - 1, 3)
                        low(u + 1, 1)
                        low(u + 1, 2)

            def layer0_rest(n, incoming):
                half = (CHUNKS // 2 - 1) // 2
                layer0_middle(n, 0, half)
                if incoming:
                    stage_last(n + 1)
                layer0_middle(n, half, CHUNKS // 2 - 1)
                u, stage = UNITS * n + LAST, LAYERS * n + 1
                aggregate_early(0)
                add(u - 1, LAST - 1, 0)
                stats_of_sum(u - 1, LAST - 1, 0)
                add(u - 1, LAST - 1, 1)
                low(u, KT - 1)
                add(u - 1, LAST - 1, 2)
                add(u - 1, LAST - 1, 3)
                stats_of_sum(u - 1, LAST - 1, 1)
                add(u, LAST, 0)
                stats_of_sum(u, LAST, 0)
                keep_early(stage)
                channel_moments(stage, 0, 0)
                stats_of_sum(u - 1, LAST - 1, 2)
                group_variance(stage, 0)
                add(u, LAST, 1)
                stats_of_sum(u, LAST, 1)
                channel_moments(stage, 1, 0)
                stats_of_sum(u - 1, LAST - 1, 3)
                group_variance(stage, 1)
                low(u + 1, 0)
                add(u, LAST, 2)
                stats_of_sum(u, LAST, 2)
                channel_moments(stage, 2, 0)
                low(u + 1, 1)
                group_variance(stage, 2)
                add(u, LAST, 3)
                stats_of_sum(u, LAST, 3)
                channel_moments(stage, 3, 0)
                low(u + 1, 2)
                group_variance(stage, 3)

            def layer1(n, incoming):
                first_unit(UNITS * n + CHUNKS, n, 1)
                for c in range(1, LAST):
                    u, h = UNITS * n + CHUNKS + c, (c - 1) % 2
                    turn_out(u - 1, n, c - 1, h, 0)
                    low(u, KT - 1)
                    if incoming:
                        turn_in(n + 1, c - 1, h, 0)
                    turn_out(u - 1, n, c - 1, h, 1)
                    if incoming:
                        turn_in(n + 1, c - 1, h, 1)
                        stats_of_input(n + 1, c - 1, 0)
                    low(u + 1, 0)
                    turn_out(u - 1, n, c - 1, h, 2)
                    if incoming:
                        turn_in(n + 1, c - 1, h, 2)
                        stats_of_input(n + 1, c - 1, 1)
                    low(u + 1, 1)
                    turn_out(u - 1, n, c - 1, h, 3)
                    if incoming:
                        turn_in(n + 1, c - 1, h, 3)
                        stats_of_input(n + 1, c - 1, 2)
                    low(u + 1, 2)
                    if incoming:
                        stats_of_input(n + 1, c - 1, 3)
                u, stage = UNITS * n + CHUNKS + LAST, LAYERS * (n + 1)
                if not incoming:
                    turn_out(u - 1, n, LAST - 1, 0, 0)
                    low(u, KT - 1)
                    for o in range(1, KT):
                        turn_out(u - 1, n, LAST - 1, 0, o)
                    for o in range(KT):
                        turn_out(u, n, LAST, 1, o)
                    return
                low(u, KT - 1)
                aggregate_early(1)
                turn_out(u - 1, n, LAST - 1, 0, 0)
                keep_early(stage)
                for k in range(KT):
                    if k == 1:
                        turn_out(u - 1, n, LAST - 1, 0, 1)
                        group_variance(stage, 0)
                    elif k == 2:
                        turn_out(u - 1, n, LAST - 1, 0, 2)
                        group_variance(stage, 1)
                        low(u + 1, 0)
                    elif k == 3:
                        low(u + 1, 1)
                        group_variance(stage, 2)
                    turn_in(n + 1, LAST - 1, 0, k)
                    stats_of_input(n + 1, LAST - 1, k)
                    channel_moments(stage, k, 1)
                low(u + 1, 2)
                group_variance(stage, 3)
                turn_out(u - 1, n, LAST - 1, 0, 3)

            dve.sem_inc(turned_out, BASE)
            for c in (0, 3, 1, 2, 6, 4, 5, 9, 7, 8, 12, 10, 11, 13):
                if c % 3 == 0:
                    first_turn_in(c)
                for k in range(KT):
                    first_stats(c, k)
            aggregate_early(1)
            first_turn_in(LAST)
            for k in range(KT):
                if k == 0:
                    keep_early(0)
                first_stats(LAST - 1, k)
                if k:
                    group_variance(0, k - 1)
                first_stats(LAST, k)
                channel_moments(0, k, 1)
                if k:
                    low(0, k - 1)
            group_variance(0, KT - 1)
            first_unit(0, 0, 0, first=True)
            dve.wait_ge(w_split, LAYERS * QUADS)
            with dve.Fori(0, IMAGES - 1) as n:
                layer0_rest(n, True)
                layer1(n, True)
                first_unit(UNITS * (n + 1), n + 1, 0)
            layer0_rest(IMAGES - 1, False)
            layer1(IMAGES - 1, False)


def kernel(**inputs):
    import numpy as _np
    import concourse.bacc as _bacc
    from concourse import mybir as _mybir
    from concourse.bass_utils import run_bass_kernel_spmd as _run

    nc = _bacc.Bacc("TRN2", target_bir_lowering=False, num_devices=1, dynamic_dma_scratch_size=1024)
    arrays, args = {}, []
    for name in ("x", "L0_conv_W", "L0_conv_b", "L1_conv_W", "L1_conv_b"):
        a = _np.ascontiguousarray(inputs[name])
        arrays[f"in_{name}"] = a
        args.append(nc.dram_tensor(f"in_{name}", a.shape, _mybir.dt.from_np(a.dtype), kind="ExternalInput").ap())
    shape = (IMAGES, HEIGHT, WIDTH, CHANNELS)
    args.append(nc.dram_tensor("out", shape, _mybir.dt.float32, kind="ExternalOutput").ap())
    preact_conv_stack(nc, *args)
    result = _run(nc, [arrays], core_ids=[0])
    return result.results[0]["out"]
```
